# Optimizing a Trainium2 kernel written in Bass

```python
import numpy as np
import jax
import jax.numpy as jnp

def _softmax(x, axis=-1):
    return jax.nn.softmax(x, axis=axis)

def _gelu(x):
    return jax.nn.gelu(x, approximate=True)

def _silu(x):
    return jax.nn.silu(x)

def _sigmoid(x):
    return jax.nn.sigmoid(x)

def _layernorm(x, axis=-1, eps=1e-05):
    m = jnp.mean(x, axis=axis, keepdims=True)
    v = jnp.var(x, axis=axis, keepdims=True)
    return (x - m) / jnp.sqrt(v + eps)

def _scatter_add(tgt, idx, src, axis=0):
    return tgt.at[idx].add(src)

def _segment_sum(src, seg, n):
    return jax.ops.segment_sum(src, seg, n)
kernel_name = 'mk_gnn_resnorm_d1_gnn_r64_645920'

def setup_inputs(seed: int=0):
    np.random.seed(seed)
    _w = jnp.asarray

    def _rec_inputs():
        import jax
        import jax.numpy as jnp
        _gk = jax.random.key(seed)
        x = -0.0003713 + 1 * jax.random.normal(jax.random.fold_in(_gk, 1), (50000, 256), jnp.float32)
        src = jax.random.randint(jax.random.fold_in(_gk, 2), (12500,), 0, 50000, jnp.int32)
        dst = jnp.minimum((50000 * jax.random.uniform(jax.random.fold_in(_gk, 3), (12500,)) ** 2.0).astype(jnp.int32), 49999)
        _o = jnp.argsort(dst, stable=True)
        src = src[_o]
        dst = dst[_o]
        edge_attr_256 = -8.16379e-05 + 0.999858 * jax.random.normal(jax.random.fold_in(_gk, 11), (12500, 256), jnp.float32)
        return (x, src, dst, edge_attr_256)
    x, src, dst, edge_attr_256 = _rec_inputs()

    def _L0_gnn_setup():
        import jax, jax.numpy as jnp
        import numpy as np
        import math
        N_NODES = 50000
        N_EDGES = 6250
        D = 256
        H = 4
        HD = D // H

        def _layernorm(x, g, b, eps=1e-05):
            mu = jnp.mean(x, axis=-1, keepdims=True)
            var = jnp.mean((x - mu) ** 2, axis=-1, keepdims=True)
            return (x - mu) * jax.lax.rsqrt(var + eps) * g + b
        key = jax.random.key(seed)
        ks = jax.random.split(key, 16)
        init = lambda k, sh: jax.random.normal(k, sh, dtype=jnp.float32) * 0.02
        inp = {'h_n': jax.random.normal(ks[0], (N_NODES, D), dtype=jnp.float32), 'h_e': jax.random.normal(ks[1], (N_EDGES, D), dtype=jnp.float32), 'edge_index': jax.random.randint(ks[2], (2, N_EDGES), 0, N_NODES, dtype=jnp.int64), 'Wq_w': init(ks[3], (2 * D, D)), 'Wq_b': jnp.zeros((D,), jnp.float32), 'Wkv_w': init(ks[4], (2 * D, 2 * D)), 'Wkv_b': jnp.zeros((2 * D,), jnp.float32), 'Wo_w': init(ks[5], (D, D)), 'Wo_b': jnp.zeros((D,), jnp.float32), 'ln1_g': jnp.ones((D,), jnp.float32), 'ln1_b': jnp.zeros((D,), jnp.float32), 'ffn1_w': init(ks[6], (D, 4 * D)), 'ffn1_b': jnp.zeros((4 * D,), jnp.float32), 'ffn2_w': init(ks[7], (4 * D, D)), 'ffn2_b': jnp.zeros((D,), jnp.float32), 'ln2_g': jnp.ones((D,), jnp.float32), 'ln2_b': jnp.zeros((D,), jnp.float32)}
        return inp
    _L0_gnn_all = _L0_gnn_setup()
    _L0_gnn_in = {k: v for k, v in _L0_gnn_all.items() if k in ('Wq_w', 'Wq_b', 'Wkv_w', 'Wkv_b', 'Wo_w', 'Wo_b', 'ln1_g', 'ln1_b', 'ffn1_w', 'ffn1_b', 'ffn2_w', 'ffn2_b', 'ln2_g', 'ln2_b')}
    del _L0_gnn_all
    return {'x': x, 'src': src, 'dst': dst, 'edge_attr_256': edge_attr_256, 'L0_gnn_Wq_w': _L0_gnn_in['Wq_w'], 'L0_gnn_Wq_b': _L0_gnn_in['Wq_b'], 'L0_gnn_Wkv_w': _L0_gnn_in['Wkv_w'], 'L0_gnn_Wkv_b': _L0_gnn_in['Wkv_b'], 'L0_gnn_Wo_w': _L0_gnn_in['Wo_w'], 'L0_gnn_Wo_b': _L0_gnn_in['Wo_b'], 'L0_gnn_ln1_g': _L0_gnn_in['ln1_g'], 'L0_gnn_ln1_b': _L0_gnn_in['ln1_b'], 'L0_gnn_ffn1_w': _L0_gnn_in['ffn1_w'], 'L0_gnn_ffn1_b': _L0_gnn_in['ffn1_b'], 'L0_gnn_ffn2_w': _L0_gnn_in['ffn2_w'], 'L0_gnn_ffn2_b': _L0_gnn_in['ffn2_b'], 'L0_gnn_ln2_g': _L0_gnn_in['ln2_g'], 'L0_gnn_ln2_b': _L0_gnn_in['ln2_b']}

def reference(x, src, dst, edge_attr_256, L0_gnn_Wq_w, L0_gnn_Wq_b, L0_gnn_Wkv_w, L0_gnn_Wkv_b, L0_gnn_Wo_w, L0_gnn_Wo_b, L0_gnn_ln1_g, L0_gnn_ln1_b, L0_gnn_ffn1_w, L0_gnn_ffn1_b, L0_gnn_ffn2_w, L0_gnn_ffn2_b, L0_gnn_ln2_g, L0_gnn_ln2_b):
    import jax
    import jax.numpy as jnp

    def _L0_gnn_ref(h_n, h_e, edge_index, Wq_w, Wq_b, Wkv_w, Wkv_b, Wo_w, Wo_b, ln1_g, ln1_b, ffn1_w, ffn1_b, ffn2_w, ffn2_b, ln2_g, ln2_b):
        import jax, jax.numpy as jnp
        import numpy as np
        import math
        N_NODES = 50000
        N_EDGES = 6250
        D = 256
        H = 4
        HD = D // H

        def _layernorm(x, g, b, eps=1e-05):
            mu = jnp.mean(x, axis=-1, keepdims=True)
            var = jnp.mean((x - mu) ** 2, axis=-1, keepdims=True)
            return (x - mu) * jax.lax.rsqrt(var + eps) * g + b
        num_nodes = h_n.shape[0]
        src, dst = (edge_index[0], edge_index[1])
        q_input = jnp.concatenate([h_n[src], h_e], axis=-1)
        kv_input = jnp.concatenate([h_n[dst], h_e], axis=-1)
        Q = q_input @ Wq_w + Wq_b
        KV = kv_input @ Wkv_w + Wkv_b
        K, V = (KV[:, :D], KV[:, D:])
        Q = Q.reshape(-1, H, HD)
        K = K.reshape(-1, H, HD)
        V = V.reshape(-1, H, HD)
        scores = jnp.sum(Q * K, axis=-1) / math.sqrt(HD)
        m = jax.ops.segment_max(scores, src, num_segments=num_nodes)
        ex = jnp.exp(scores - m[src])
        denom = jax.ops.segment_sum(ex, src, num_segments=num_nodes)
        attn = ex / denom[src]
        wv = attn[:, :, None] * V
        out = jax.ops.segment_sum(wv, src, num_segments=num_nodes)
        out = out.reshape(num_nodes, D)
        out = out @ Wo_w + Wo_b
        h = _layernorm(h_n + out, ln1_g, ln1_b)
        ff = jax.nn.gelu(h @ ffn1_w + ffn1_b, approximate=False) @ ffn2_w + ffn2_b
        h = _layernorm(h + ff, ln2_g, ln2_b)
        return h
    edge_index = jnp.stack([src, dst])
    x = _layernorm(x + _L0_gnn_ref(x, edge_attr_256, edge_index, L0_gnn_Wq_w, L0_gnn_Wq_b, L0_gnn_Wkv_w, L0_gnn_Wkv_b, L0_gnn_Wo_w, L0_gnn_Wo_b, L0_gnn_ln1_g, L0_gnn_ln1_b, L0_gnn_ffn1_w, L0_gnn_ffn1_b, L0_gnn_ffn2_w, L0_gnn_ffn2_b, L0_gnn_ln2_g, L0_gnn_ln2_b), axis=-1)
    return x

_drawn_inputs = setup_inputs


def setup_inputs(seed=0):
    import zlib

    import numpy as np

    out = dict(_drawn_inputs(seed))
    spreads = {'L0_gnn_Wq_b': (0.0, 0.8),
     'L0_gnn_Wkv_b': (0.0, 0.8),
     'L0_gnn_Wo_b': (0.0, 0.1),
     'L0_gnn_ln1_g': (1.0, 0.2),
     'L0_gnn_ln1_b': (0.0, 0.1),
     'L0_gnn_ffn1_b': (0.0, 0.437),
     'L0_gnn_ffn2_b': (0.0, 0.1),
     'L0_gnn_ln2_g': (1.0, 0.2),
     'L0_gnn_ln2_b': (0.0, 0.1)}
    factors = {'L0_gnn_Wq_w': 8.0}
    for name, (base, spread) in spreads.items():
        noise = np.random.default_rng([zlib.crc32(name.encode()), seed]).standard_normal(out[name].shape)
        drawn = base * np.exp(spread * noise) if base else spread * noise
        out[name] = jnp.asarray(drawn.astype(out[name].dtype))
    for name, factor in factors.items():
        out[name] = (out[name] * factor).astype(out[name].dtype)
    return out
```

```python
from contextlib import ExitStack

import concourse.bass as bass
from concourse import mybir

F32 = mybir.dt.float32
F32R = mybir.dt.float32r
BF16 = mybir.dt.bfloat16
I32 = mybir.dt.int32
ALU = mybir.AluOpType
ACT = mybir.ActivationFunctionType

P = 128
D = 256
KD = D // P
FF = 4 * D
NF = FF // P
HEADS = 4
HD = D // HEADS
N_NODES = 50000
N_EDGES = 12500
EPS = 1e-5

T = 100
E_PAD = P * T
E_ROWS = N_EDGES // T
RADIX = 256
PAD_KEY = RADIX * RADIX - 1
NO_EDGE = 60000
CH = 10
NCH = T // CH
SEEN = 5
BIG = 3.0e38

J = 4
GE = J * P
NGE = E_PAD // GE
NC = 3 * KD

GN = J * P
NG = -(-N_NODES // GN)
TAIL = (N_NODES - (NG - 1) * GN) // J
RING = 4

assert E_ROWS * T == N_EDGES and NGE * GE == E_PAD and TAIL * J == N_NODES - (NG - 1) * GN


def level(eng, v):
    return v if isinstance(v, int) else eng.snap(eng.to_reg(v))


def build(nc, x, src, dst, edge_attr, wq, bq, wkv, bkv, wo, bo, ln1_g, ln1_b, w1, b1, w2, b2, ln2_g, ln2_b, out):
    rows_by_low = nc.dram_tensor("rows_by_low", (E_PAD, 3), I32).ap()
    rows_sorted = nc.dram_tensor("rows_sorted", (E_PAD, 3), I32).ap()
    penalty_row = nc.dram_tensor("penalty_row", (E_PAD,), F32).ap()
    place_of_node = nc.dram_tensor("place_of_node", (RADIX * RADIX,), I32).ap()
    attn_rows = nc.dram_tensor("attn_rows", (E_PAD, D), F32).ap()

    with ExitStack() as keep:
        def sb(name, shape, dt=F32):
            return keep.enter_context(nc.sbuf_tensor(name, shape, dt))

        ident = sb("ident", [P, P])
        head_sum = sb("head_sum", [P, P])
        ones = sb("ones", [P, P])
        wts = {}
        for name, k, n in (("q", 2 * KD, D), ("kv", 2 * KD, 2 * D), ("o", KD, D), ("1", KD, FF), ("2", NF, D)):
            wts[name] = (sb(f"w{name}_hi", [P, k, n], F32R), sb(f"w{name}_lo", [P, k, n], F32R))
        bq_c = sb("bq_c", [P, KD])
        bkv_c = sb("bkv_c", [P, 2 * KD])
        b1_c = sb("b1_c", [P, NF])
        b2_c = sb("b2_c", [P, KD])
        g1_c = sb("g1_c", [P, KD])
        be1_c = sb("be1_c", [P, KD])
        bo_r = sb("bo_r", [P, D])
        g2_r = sb("g2_r", [P, D])
        be2_r = sb("be2_r", [P, D])
        edge_idx = sb("edge_idx", [P, T, 3], I32)

        sort_stage(nc, src, dst, wq, wkv, wo, w1, w2,
                   ((bq_c, bq), (bkv_c, bkv), (b1_c, b1), (b2_c, b2), (g1_c, ln1_g), (be1_c, ln1_b)),
                   ((bo_r, bo), (g2_r, ln2_g), (be2_r, ln2_b)),
                   wts, ident, head_sum, ones, edge_idx, rows_by_low, rows_sorted, penalty_row, place_of_node)
        edge_stage(nc, x, edge_attr, wts, ident, head_sum, bq_c, bkv_c, bo_r, edge_idx, penalty_row, attn_rows)
        node_stage(nc, x, wts, ident, b1_c, b2_c, g1_c, be1_c, bo_r, g2_r, be2_r, place_of_node, attn_rows, out)


def sort_stage(nc, src, dst, wq, wkv, wo, w1, w2, columns, broadcasts, wts, ident, head_sum, ones, edge_idx,
               rows_by_low, rows_sorted, penalty_row, place_of_node):
    with ExitStack() as ctx:
        def sb(name, shape, dt=F32):
            return ctx.enter_context(nc.sbuf_tensor(name, shape, dt))

        def pb(name, shape):
            return ctx.enter_context(nc.psum_tensor(name, shape, F32))

        def sem(name):
            return ctx.enter_context(nc.semaphore(name))

        src_t = sb("src_t", [P, T], I32)
        dst_t = sb("dst_t", [P, T], I32)
        eid_t = sb("eid_t", [P, T], I32)
        rows = sb("rows", [P, T, 3], I32)
        prev = sb("prev", [P, T], I32)
        low_i = sb("low_i", [P, T], I32)
        high_i = sb("high_i", [P, T], I32)
        low = sb("low", [P, T])
        high = sb("high", [P, T])
        hot = sb("hot", [P, 2, CH * RADIX], BF16)
        hot_low = sb("hot_low", [P, 2, CH * RADIX], BF16)
        iota_i = sb("iota_i", [P, RADIX], I32)
        iota = sb("iota", [P, RADIX], BF16)
        zeros = sb("zeros", [P, RADIX])
        tri_bf = sb("tri_bf", [P, P], BF16)
        ones_bf = sb("ones_bf", [P, P], BF16)
        tri = sb("tri", [P, P])
        seen = sb("seen", [P, SEEN, RADIX])
        upto = sb("upto", [P, 2, RADIX])
        junk = sb("junk", [P, 2, RADIX], BF16)
        rank = sb("rank", [P, 2, CH])
        rank_st = sb("rank_st", [P, 2, CH], I32)
        rows_st = sb("rows_st", [P, 2, CH, 3], I32)
        totals = sb("totals", [P, 2])
        before = sb("before", [P, 2])
        empty = sb("empty", [P, 2, RADIX])
        place = sb("place", [P, 2, RADIX])
        place_i = sb("place_i", [P, 2, RADIX], I32)
        same = sb("same", [P, T])
        penalty = sb("penalty", [P, T])
        stage = {n: sb(f"st_{n}", list(wts[n][0].shape)) for n in wts}
        p_lanes = pb("p_lanes", [P, 2, RADIX])
        p_total = pb("p_total", [P, 2, RADIX])
        p_hist = [pb(f"p_hist{i}", [P, RADIX]) for i in range(2)]
        p_before = pb("p_before", [P, 2])

        s_in = sem("s_in")
        s_eid = sem("s_eid")
        s_pad = sem("s_pad")
        s_zero = sem("s_zero")
        s_const = sem("s_const")
        s_w = {n: sem(f"s_w{n}") for n in wts}
        s_whi = sem("s_whi")
        s_wlo = sem("s_wlo")
        s_small = sem("s_small")
        s_iota = sem("s_iota")
        s_rows = sem("s_rows")
        s_int = sem("s_int")
        s_digit = sem("s_digit")
        s_hot = [sem(f"s_hot{i}") for i in range(2)]
        s_again = [sem(f"s_again{i}") for i in range(2)]
        s_cnt = [sem(f"s_cnt{i}") for i in range(2)]
        s_base = [sem(f"s_base{i}") for i in range(2)]
        s_seen = [sem(f"s_seen{i}") for i in range(2)]
        s_rank = [sem(f"s_rank{i}") for i in range(2)]
        s_staged = [sem(f"s_staged{i}") for i in range(2)]
        s_scat = [[sem(f"s_scat{i}{u}") for u in range(2)] for i in range(2)]
        s_reload = sem("s_reload")
        s_final = sem("s_final")
        s_prev0 = sem("s_prev0")
        s_prev = sem("s_prev")
        s_pen = sem("s_pen")
        s_tot = sem("s_tot")
        s_bef = sem("s_bef")
        s_place = sem("s_place")
        s_put = sem("s_put")

        w_dram = {"q": wq, "kv": wkv, "o": wo, "1": w1, "2": w2}
        block = ctx.enter_context(nc.Block())

        @block.sync
        def _(sp):
            sp.wait_ge(s_pad, 2)
            sp.dma_start(src_t[0:E_ROWS, :], src.rearrange("(p t) -> p t", t=T)).then_inc(s_in, 16)
            sp.dma_start(dst_t[0:E_ROWS, :], dst.rearrange("(p t) -> p t", t=T)).then_inc(s_in, 16)
            for n, w in w_dram.items():
                sp.dma_start(stage[n][:], w.rearrange("(k p) n -> p k n", p=P)).then_inc(s_w[n], 16)
            for tile, v in columns:
                sp.dma_start(tile[:], v.rearrange("(k p) -> p k", p=P),
                             allow_slow_non_contiguous=True).then_inc(s_small, 16)
            for tile, v in broadcasts:
                sp.dma_start(tile[:], v.partition_broadcast(P)).then_inc(s_small, 16)
            for u in range(2):
                sp.wait_ge(s_scat[0][u], 16 * T // 2)
            sp.dma_start(rows[:], rows_by_low.rearrange("(p t) c -> p t c", t=T)).then_inc(s_reload, 16)
            for u in range(2):
                sp.wait_ge(s_scat[1][u], 16 * T // 2)
            sp.dma_start(rows[:], rows_sorted.rearrange("(p t) c -> p t c", t=T)).then_inc(s_final, 16)
            sp.dma_start(edge_idx[:], rows_sorted.rearrange("(t p) c -> p t c", p=P)).then_inc(s_final, 16)
            sp.wait_ge(s_prev0, 1)
            sp.dma_start(prev[1:P, 0:1],
                         rows_sorted.rearrange("(p t) c -> p t c", t=T)[0:P - 1, T - 1, 0:1],
                         allow_slow_non_contiguous=True).then_inc(s_final, 16)
            sp.wait_ge(s_place, 7)
            for c in range(2):
                sp.dma_start(place_of_node[c * P * RADIX:(c + 1) * P * RADIX].rearrange("(p n) -> p n", n=RADIX),
                             place_i[:, c, :]).then_inc(s_put, 16)
            sp.wait_ge(s_pen, 2)
            sp.dma_start(penalty_row.rearrange("(p t) -> p t", t=T), penalty[:]).then_inc(s_put, 16)
            sp.wait_ge(s_put, 48)
            sp.wait_ge(s_small, 16 * (len(columns) + len(broadcasts)))

        @block.gpsimd
        def _(pool):
            pool.memset(src_t[:], PAD_KEY).then_inc(s_pad, 1)
            pool.memset(dst_t[:], 0).then_inc(s_pad, 1)
            pool.iota(iota_i[:], pattern=[[1, RADIX]], base=0, channel_multiplier=0).then_inc(s_iota, 1)
            pool.iota(eid_t[:], pattern=[[1, T]], base=0, channel_multiplier=T).then_inc(s_eid, 1)
            pool.memset(ones[:], 1.0).then_inc(s_zero, 1)
            pool.memset(ones_bf[:], 1.0).then_inc(s_zero, 1)
            pool.memset(zeros[:], 0.0).then_inc(s_zero, 1)
            pool.memset(head_sum[:], 0.0).then_inc(s_zero, 1)
            pool.memset(ident[:], 0.0).then_inc(s_zero, 1)
            pool.memset(prev[:], -1).then_inc(s_prev0, 1)
            pool.wait_ge(s_zero, 5)
            pool.affine_select(out=tri_bf[:], in_=ones_bf[:], compare_op=ALU.is_gt, fill=0.0, base=0,
                               pattern=[[1, P]], channel_multiplier=-1).then_inc(s_const, 1)
            pool.affine_select(out=tri[:], in_=ones[:], compare_op=ALU.is_gt, fill=0.0, base=0,
                               pattern=[[1, P]], channel_multiplier=-1).then_inc(s_const, 1)
            pool.affine_select(out=ident[:], in_=ident[:], compare_op=ALU.not_equal, fill=1.0, base=0,
                               pattern=[[-1, P]], channel_multiplier=1).then_inc(s_const, 1)
            for h in range(P // HD):
                pool.wait_ge(s_const, 3 + h)
                pool.memset(head_sum[h * HD:(h + 1) * HD, h * HD:(h + 1) * HD], HD ** -0.5).then_inc(s_const, 1)

            def scatter(i, c, u):
                n_staged = level(pool, 2 * c + 2)
                pool.wait_ge(s_const, 5)
                pool.wait_ge(s_staged[i], n_staged)
                for j in range(CH):
                    pool.indirect_dma_start(
                        (rows_by_low, rows_sorted)[i],
                        bass.IndirectOffsetOnAxis(ap=rank_st[:, u, j:j + 1], axis=0),
                        rows_st[:, u, j, :], None).then_inc(s_scat[i][u], 16)

            for i in range(2):
                with pool.Fori(0, NCH // 2) as h:
                    scatter(i, 2 * h, 0)
                    scatter(i, 2 * h + 1, 1)

        @block.scalar
        def _(act):
            for n in wts:
                act.wait_ge(s_w[n], 16)
                act.activation(wts[n][0][:], stage[n][:], ACT.Copy).then_inc(s_whi, 1)

            def stage_step(i, h, u, first):
                c = 2 * h + u
                act.wait_ge(s_rank[i], CH * c + CH)
                if not first:
                    act.wait_ge(s_scat[i][u], 16 * CH * h)
                elif i:
                    act.wait_ge(s_scat[0][u], 16 * T // 2)
                act.activation(rank_st[:, u, :], rank[:, u, :], ACT.Copy).then_inc(s_staged[i], 1)
                act.activation(rows_st[:, u, :, :], rows[:, bass.ds(c * CH, CH), :], ACT.Copy).then_inc(s_staged[i], 1)

            for i in range(2):
                for u in range(2):
                    stage_step(i, 0, u, True)
                with act.Fori(1, NCH // 2) as h:
                    for u in range(2):
                        stage_step(i, h, u, False)

        @block.tensor
        def _(pe):
            pe.wait_ge(s_const, 5)

            def count(i, c, u, first, last):
                pe.wait_ge(s_hot[i], c + 1)
                for j in range(CH):
                    start, stop = first and j == 0, last and j == CH - 1
                    one = hot[:, u, j * RADIX:(j + 1) * RADIX]
                    pe.matmul(p_lanes[:, i, :], tri_bf[:], one, start=start, stop=stop)
                    mm = pe.matmul(p_total[:, i, :], ones_bf[:], one, start=start, stop=stop)
                    if i:
                        for h in range(2):
                            mm = pe.matmul(p_hist[h][:],
                                           hot[:, u, j * RADIX + h * P:j * RADIX + (h + 1) * P],
                                           hot_low[:, u, j * RADIX:(j + 1) * RADIX], start=start, stop=stop)
                mm.then_inc(s_cnt[i], 1)

            for i in range(2):
                count(i, 0, 0, True, False)
                count(i, 1, 1, False, False)
                with pe.Fori(1, NCH // 2 - 1) as h:
                    count(i, 2 * h, 0, False, False)
                    count(i, 2 * h + 1, 1, False, False)
                count(i, NCH - 2, 0, False, False)
                count(i, NCH - 1, 1, False, True)
            pe.wait_ge(s_tot, 1)
            pe.matmul(p_before[:, 0:1], tri[:], totals[:, 0:1], start=True, stop=True)
            pe.matmul(p_before[:, 1:2], tri[:], totals[:, 1:2], start=True, stop=False)
            pe.matmul(p_before[:, 1:2], ones[:], totals[:, 0:1], start=False, stop=True).then_inc(s_bef, 1)

        @block.vector
        def _(dve):
            dve.wait_ge(s_iota, 1)
            dve.tensor_copy(iota[:], iota_i[:]).then_inc(s_iota, 1)
            dve.wait_ge(s_in, 32)
            dve.tensor_copy(rows[:, :, 0], src_t[:]).then_inc(s_rows, 1)
            dve.tensor_copy(rows[:, :, 1], dst_t[:]).then_inc(s_rows, 1)
            dve.wait_ge(s_eid, 1)
            dve.tensor_scalar(rows[:, :, 2], eid_t[:], float(N_EDGES - 1), None, ALU.min).then_inc(s_rows, 1)
            dve.wait_ge(s_rows, 3)

            def digits(n):
                dve.tensor_single_scalar(low_i[:], rows[:, :, 0], RADIX - 1, ALU.bitwise_and).then_inc(s_int, 1)
                dve.tensor_single_scalar(high_i[:], rows[:, :, 0], 8, ALU.logical_shift_right).then_inc(s_int, 1)
                dve.wait_ge(s_int, 2 * n)
                dve.tensor_copy(low[:], low_i[:]).then_inc(s_digit, 1)
                dve.tensor_copy(high[:], high_i[:]).then_inc(s_digit, 1)
                dve.wait_ge(s_digit, 2 * n)

            def one_hot(i, c, u, used):
                if used:
                    dve.wait_ge(s_cnt[i], c - 1)
                for j in range(CH):
                    if i:
                        dve.tensor_scalar(hot_low[:, u, j * RADIX:(j + 1) * RADIX], iota[:],
                                          low[:, bass.ds(c * CH + j, 1)], None, ALU.is_equal)
                    op = dve.tensor_scalar(hot[:, u, j * RADIX:(j + 1) * RADIX], iota[:],
                                           (low, high)[i][:, bass.ds(c * CH + j, 1)], None, ALU.is_equal)
                op.then_inc(s_hot[i], 1)

            def count_seen(i, h, u, first):
                c = 2 * h + u
                if not first:
                    dve.wait_ge(s_rank[i], CH * c - CH)
                    dve.wait_ge(s_seen[i], CH * c - CH)
                    dve.wait_ge(s_staged[i], 2 * c - 2)
                elif i:
                    dve.wait_ge(s_staged[0], 2 * NCH)
                for j in range(CH):
                    op = dve.tensor_scalar(hot[:, u, j * RADIX:(j + 1) * RADIX], iota[:],
                                           (low, high)[i][:, bass.ds(c * CH + j, 1)], None, ALU.is_equal)
                op.then_inc(s_again[i], 1)
                dve.wait_ge(s_again[i], c + 1)
                for j in range(CH):
                    one = hot[:, u, j * RADIX:(j + 1) * RADIX]
                    dve.wait_ge(s_seen[i], c * CH + j + 1)
                    if not (first and u == 0 and j < 2):
                        dve.wait_ge(s_rank[i], c * CH + j - 1)
                    dve.tensor_tensor(seen[:, (j + 1) % SEEN, :], seen[:, j % SEEN, :], one,
                                      ALU.add).then_inc(s_seen[i], 1)
                    dve.tensor_tensor_reduce(out=junk[:, j % 2, :], in0=seen[:, j % SEEN, :], in1=one, scale=1.0,
                                             scalar=0.0, op0=ALU.mult, op1=ALU.add,
                                             accum_out=rank[:, u, j:j + 1]).then_inc(s_rank[i], 1)

            for i in range(2):
                if i:
                    dve.wait_ge(s_reload, 16)
                digits(i + 1)
                if i:
                    dve.wait_ge(s_rank[0], T)
                    dve.wait_ge(s_seen[0], T + 1)
                else:
                    dve.wait_ge(s_iota, 2)
                one_hot(i, 0, 0, False)
                one_hot(i, 1, 1, False)
                with dve.Fori(1, NCH // 2) as h:
                    one_hot(i, 2 * h, 0, True)
                    one_hot(i, 2 * h + 1, 1, True)
                dve.wait_ge(s_cnt[i], NCH)
                dve.wait_ge(s_zero, 5)
                dve.tensor_tensor_scan(upto[:, 0, :], p_total[:, i, :], zeros[:], 0.0, ALU.add,
                                       ALU.add).then_inc(s_base[i], 1)
                dve.wait_ge(s_base[i], 1)
                dve.tensor_tensor(upto[:, 1, :], upto[:, 0, :], p_total[:, i, :], ALU.subtract).then_inc(s_base[i], 1)
                dve.wait_ge(s_base[i], 2)
                dve.tensor_tensor(seen[:, 0, :], upto[:, 1, :], p_lanes[:, i, :], ALU.add).then_inc(s_seen[i], 1)
                for u in range(2):
                    count_seen(i, 0, u, True)
                with dve.Fori(1, NCH // 2) as h:
                    for u in range(2):
                        count_seen(i, h, u, False)

            dve.wait_ge(s_seen[1], T + 1)
            for h in range(2):
                dve.tensor_tensor_scan(upto[:, h, :], p_hist[h][:], zeros[:], 0.0, ALU.add,
                                       ALU.add).then_inc(s_place, 1)
                dve.tensor_scalar(empty[:, h, :], p_hist[h][:], 0.0, float(NO_EDGE), ALU.is_equal,
                                  ALU.mult).then_inc(s_place, 1)
            dve.wait_ge(s_place, 4)
            dve.tensor_copy(totals[:], upto[:, :, RADIX - 1]).then_inc(s_tot, 1)
            dve.wait_ge(s_bef, 1)
            dve.tensor_scalar(before[:], p_before[:], -1.0, None, ALU.add).then_inc(s_bef, 1)
            dve.wait_ge(s_bef, 2)
            for h in range(2):
                op = dve.scalar_tensor_tensor(out=place[:, h, :], in0=upto[:, h, :], scalar=before[:, h:h + 1],
                                              in1=empty[:, h, :], op0=ALU.add, op1=ALU.add)
                op.then_inc(s_place, 1)
            dve.wait_ge(s_place, 6)
            dve.tensor_copy(place_i[:], place[:]).then_inc(s_place, 1)

            for n, w in enumerate(wts):
                dve.wait_ge(s_whi, n + 1)
                dve.tensor_tensor(wts[w][1][:], stage[w][:], wts[w][0][:].bitcast(F32), ALU.subtract).then_inc(s_wlo, 1)

            dve.wait_ge(s_final, 48)
            dve.tensor_copy(prev[:, 1:T], rows[:, 0:T - 1, 0]).then_inc(s_prev, 1)
            dve.tensor_scalar(edge_idx[:], edge_idx[:], float(N_NODES - 1), None, ALU.min)
            dve.wait_ge(s_prev, 1)
            dve.tensor_tensor(same[:], rows[:, :, 0], prev[:], ALU.is_equal).then_inc(s_pen, 1)
            dve.wait_ge(s_pen, 1)
            dve.tensor_scalar(penalty[:], same[:], -1.0, BIG, ALU.add, ALU.mult).then_inc(s_pen, 1)


def edge_stage(nc, x, edge_attr, wts, ident, head_sum, bq_c, bkv_c, bo_r, edge_idx, penalty_row, attn_rows):
    with ExitStack() as ctx:
        def sb(name, shape, dt=F32):
            return ctx.enter_context(nc.sbuf_tensor(name, shape, dt))

        def pb(name):
            return ctx.enter_context(nc.psum_tensor(name, [P, GE], F32))

        def sem(name):
            return ctx.enter_context(nc.semaphore(name))

        idx = sb("idx", [P, 2, J, 3], I32)
        got = sb("got", [P, 2, 3, J, D])
        in_hi = sb("in_hi", [P, 2, NC, GE], F32R)
        in_lo = sb("in_lo", [P, 2, NC, GE], F32R)
        pen = sb("pen", [P, 2, GE])
        q_sb = sb("q_sb", [P, GE])
        qk = sb("qk", [P, GE])
        top = sb("top", [P, 2, KD, GE + 1])
        fall_a = sb("fall_a", [P, GE])
        fall_b = sb("fall_b", [P, GE])
        rise = sb("rise", [P, GE])
        decay = sb("decay", [P, GE])
        prob = sb("prob", [P, GE])
        pv = sb("pv", [P, GE])
        num = sb("num", [P, 2, KD, GE])
        den = sb("den", [P, 2, KD, GE])
        att = sb("att", [P, KD, GE])
        att_hi = sb("att_hi", [P, 2, KD, GE], F32R)
        att_lo = sb("att_lo", [P, 2, KD, GE], F32R)
        y = sb("y", [P, J, D])
        p_t = [pb(f"p_t{i}") for i in range(2)]
        p_q = pb("p_q")
        p_k = pb("p_k")
        p_v = [pb(f"p_v{i}") for i in range(2)]
        p_s = pb("p_s")
        p_o = pb("p_o")

        e_idx = sem("e_idx")
        e_got = [sem(f"e_got{i}") for i in range(2)]
        e_pen = [sem(f"e_pen{i}") for i in range(2)]
        e_t = sem("e_t")
        e_hi = sem("e_hi")
        e_lo = sem("e_lo")
        e_q = sem("e_q")
        e_qs = sem("e_qs")
        e_k = sem("e_k")
        e_qk = sem("e_qk")
        e_v = sem("e_v")
        e_s = sem("e_s")
        e_top = sem("e_top")
        e_fa = sem("e_fa")
        e_fb = sem("e_fb")
        e_rise = sem("e_rise")
        e_exp = sem("e_exp")
        e_pv = sem("e_pv")
        e_num = sem("e_num")
        e_den = sem("e_den")
        e_rd = sem("e_rd")
        e_att = sem("e_att")
        e_ahi = sem("e_ahi")
        e_alo = sem("e_alo")
        e_carry = sem("e_carry")
        e_o = sem("e_o")
        e_rows = sem("e_rows")
        e_y = sem("e_y")
        e_put = sem("e_put")
        block = ctx.enter_context(nc.Block())

        wq_hi, wq_lo = wts["q"]
        wkv_hi, wkv_lo = wts["kv"]
        wo_hi, wo_lo = wts["o"]

        def live(g):
            return 0 <= g < NGE

        def over_groups(eng, body):
            for g in range(-2, 4):
                body(g, g // 2, g)
            with eng.Fori(2, (NGE - 3) // 2) as h:
                body(2 * h, h, 4)
                body(2 * h + 1, h, 5)
            for g in range((NGE - 3) // 2 * 2, NGE + 1):
                body(g, g // 2, g)

        @block.sync
        def _(sp):
            def group(g, h, g0):
                u = g0 % 2
                n_fb, n_y = sp.snap(2 * g) if not isinstance(g, int) else 2 * g, \
                    sp.snap(2 * g) if not isinstance(g, int) else 2 * g
                ahead = sp.snap(g * GE + GE) if not isinstance(g, int) else (g + 1) * GE
                behind = sp.snap(g * GE - GE) if not isinstance(g, int) else (g - 1) * GE
                if live(g0 + 1):
                    if live(g0 - 1):
                        sp.wait_ge(e_fa, n_fb)
                    sp.dma_start(pen[:, 1 - u, :],
                                 penalty_row[bass.ds(ahead, GE)].partition_broadcast(P)).then_inc(e_pen[1 - u], 16)
                if live(g0 - 1):
                    sp.wait_ge(e_y, n_y)
                    sp.dma_start(attn_rows[bass.ds(behind, GE), :].rearrange("(j p) d -> p j d", p=P),
                                 y[:]).then_inc(e_put, 16)

            over_groups(sp, group)
            sp.wait_ge(e_put, 16 * NGE)

        @block.gpsimd
        def _(pool):
            def att_low(g, g0, m):
                u = g0 % 2
                pool.wait_ge(e_ahi, 2 * g + m + 1)
                if g0 >= 2:
                    pool.wait_ge(e_o, 2 * g - 2)
                pool.tensor_tensor(att_lo[:, u, m, :], att[:, m, :], att_hi[:, u, m, :].bitcast(F32),
                                   ALU.subtract).then_inc(e_alo, 1)

            def group(g, h, g0):
                u = g0 % 2
                if live(g0 + 2):
                    if live(g0):
                        pool.wait_ge(e_got[u], 16 * 3 * J * h + 16 * 3 * J)
                    if isinstance(g, int):
                        piece = edge_idx[:, (g + 2) * J:(g + 3) * J, :]
                    else:
                        piece = edge_idx[:, bass.ds(g * J + 2 * J, J), :]
                    pool.tensor_copy(idx[:, u, :, :], piece).then_inc(e_idx, 1)
                    n_idx, n_turned = level(pool, g + 3), level(pool, NC * g + NC)
                    pool.wait_ge(e_idx, 1)
                    pool.wait_ge(e_idx, n_idx)
                    if live(g0):
                        pool.wait_ge(e_t, n_turned)
                    for k, (table, col) in enumerate(((x, 0), (x, 1), (edge_attr, 2))):
                        for j in range(J):
                            pool.indirect_dma_start(
                                got[:, u, k, j, :], None, table,
                                bass.IndirectOffsetOnAxis(ap=idx[:, u, j, col:col + 1], axis=0)
                            ).then_inc(e_got[u], 16)
                        if k == 0 and live(g0 - 1):
                            att_low(g - 1, g0 - 1, 1)
                elif live(g0 - 1):
                    att_low(g - 1, g0 - 1, 1)
                if live(g0):
                    att_low(g, g0, 0)
                if live(g0 - 1):
                    for i in range(2):
                        pool.wait_ge(e_rows, 2 * g - 2 + i + 1)
                        pool.tensor_tensor(y[:, 2 * i:2 * i + 2, :], y[:, 2 * i:2 * i + 2, :],
                                           bo_r[:].unsqueeze(1).to_broadcast([P, 2, D]), ALU.add).then_inc(e_y, 1)

            over_groups(pool, group)

        @block.tensor
        def _(pe):
            def turn(g, h, u, c):
                if c == 0:
                    pe.wait_ge(e_got[u], 16 * 3 * J * h + 16 * 3 * J)
                if not (isinstance(g, int) and g == 0 and c < 2):
                    pe.wait_ge(e_hi, NC * g + c - 1)
                    pe.wait_ge(e_lo, NC * g + c - 1)
                for j in range(J):
                    mm = pe.transpose(p_t[c % 2][:, j * P:(j + 1) * P],
                                      got[:, u, c // KD, j, (c % KD) * P:(c % KD + 1) * P], ident[:])
                mm.then_inc(e_t, 1)

            def project(bank, w_hi, w_lo, col, u, chunks, done):
                n = len(chunks)
                for k, c in enumerate(chunks):
                    hi, lo = w_hi[:, k, col:col + P], w_lo[:, k, col:col + P]
                    pe.matmul(bank, hi, in_hi[:, u, c, :], start=(k == 0), stop=False)
                    pe.matmul(bank, hi, in_lo[:, u, c, :], start=False, stop=False)
                    mm = pe.matmul(bank, lo, in_hi[:, u, c, :], start=False, stop=(k == n - 1))
                mm.then_inc(done, 1)

            def group(g, h, g0):
                u = g0 % 2
                cur, nxt = live(g0), live(g0 + 1)
                hn = h if u == 0 else h + 1
                for m in range(KD):
                    if cur:
                        if m == 0:
                            pe.wait_ge(e_hi, NC * g + NC)
                            pe.wait_ge(e_lo, NC * g + NC)
                        if g0 or m:
                            pe.wait_ge(e_qs, 2 * g + m)
                        project(p_q[:], wq_hi, wq_lo, m * P, u, (0, 1, 4, 5), e_q)
                    if nxt:
                        turn(g + 1, hn, 1 - u, 3 * m)
                    if cur:
                        if g0 or m:
                            pe.wait_ge(e_qk, 2 * g + m)
                        project(p_k[:], wkv_hi, wkv_lo, m * P, u, (2, 3, 4, 5), e_k)
                    if nxt:
                        turn(g + 1, hn, 1 - u, 3 * m + 1)
                    if cur:
                        if g0:
                            pe.wait_ge(e_pv, 2 * g + m - 1)
                        project(p_v[m][:], wkv_hi, wkv_lo, D + m * P, u, (2, 3, 4, 5), e_v)
                    if nxt:
                        turn(g + 1, hn, 1 - u, 3 * m + 2)
                    if cur:
                        if g0 or m:
                            pe.wait_ge(e_rise, 2 * g + m)
                        pe.wait_ge(e_qk, 2 * g + m + 1)
                        pe.matmul(p_s[:], head_sum[:], qk[:], start=True, stop=True).then_inc(e_s, 1)
                if live(g0 - 1):
                    pe.wait_ge(e_ahi, 2 * g)
                    pe.wait_ge(e_alo, 2 * g)
                    for i in range(2):
                        if not (isinstance(g, int) and g == 1 and i == 0):
                            pe.wait_ge(e_rows, 2 * g - 2 + i)
                        for j in (2 * i, 2 * i + 1):
                            acc = p_o[:, (j % 2) * D:(j % 2 + 1) * D]
                            for m in range(KD):
                                hi = att_hi[:, 1 - u, m, j * P:(j + 1) * P]
                                lo = att_lo[:, 1 - u, m, j * P:(j + 1) * P]
                                pe.matmul(acc, hi, wo_hi[:, m, :], start=(m == 0), stop=False)
                                pe.matmul(acc, hi, wo_lo[:, m, :], start=False, stop=False)
                                mm = pe.matmul(acc, lo, wo_hi[:, m, :], start=False, stop=(m == KD - 1))
                        mm.then_inc(e_o, 1)

            over_groups(pe, group)

        @block.scalar
        def _(act):
            def high(g, u, c):
                act.wait_ge(e_t, NC * g + c + 1)
                if not (isinstance(g, int) and g < 2):
                    act.wait_ge(e_v, 2 * g - 2)
                act.activation(in_hi[:, u, c, :], p_t[c % 2][:], ACT.Copy).then_inc(e_hi, 1)

            def att_high(g, g0, m):
                act.wait_ge(e_att, 2 * g + m + 1)
                if g0 >= 2:
                    act.wait_ge(e_o, 2 * g - 2)
                act.activation(att_hi[:, g0 % 2, m, :], att[:, m, :], ACT.Copy).then_inc(e_ahi, 1)

            def group(g, h, g0):
                u = g0 % 2
                cur, nxt = live(g0), live(g0 + 1)

                def q_out(m):
                    act.wait_ge(e_q, 2 * g + m + 1)
                    if g0 or m:
                        act.wait_ge(e_qk, 2 * g + m)
                    act.activation(q_sb[:], p_q[:], ACT.Identity, bias=bq_c[:, m:m + 1]).then_inc(e_qs, 1)

                def exps(m):
                    act.wait_ge(e_fb, 2 * g + m + 1)
                    if g0 or m:
                        act.wait_ge(e_den, 2 * g + m)
                    act.activation(decay[:], fall_b[:], ACT.Exp).then_inc(e_exp, 1)
                    act.wait_ge(e_rise, 2 * g + m + 1)
                    act.activation(prob[:], rise[:], ACT.Exp).then_inc(e_exp, 1)

                def rows_out(i):
                    act.wait_ge(e_o, 2 * g - 2 + i + 1)
                    if g0 >= 2:
                        act.wait_ge(e_put, 16 * g - 16)
                    act.activation(y[:, 2 * i:2 * i + 2, :], p_o[:].rearrange("p (j d) -> p j d", d=D),
                                   ACT.Copy).then_inc(e_rows, 1)

                if cur:
                    q_out(0)
                if nxt:
                    for c in range(3):
                        high(g + 1, 1 - u, c)
                if live(g0 - 1):
                    att_high(g - 1, g0 - 1, 1)
                if cur:
                    exps(0)
                if nxt:
                    high(g + 1, 1 - u, 3)
                if cur:
                    q_out(1)
                if nxt:
                    high(g + 1, 1 - u, 4)
                    high(g + 1, 1 - u, 5)
                if live(g0 - 1):
                    rows_out(0)
                if cur:
                    exps(1)
                    att_high(g, g0, 0)
                if live(g0 - 1):
                    rows_out(1)

            over_groups(act, group)

        @block.vector
        def _(dve):
            def low(g, u, c):
                dve.wait_ge(e_hi, NC * g + c + 1)
                dve.tensor_tensor(in_lo[:, u, c, :], p_t[c % 2][:], in_hi[:, u, c, :].bitcast(F32),
                                  ALU.subtract).then_inc(e_lo, 1)

            def group(g, h, g0):
                u = g0 % 2
                cur, nxt = live(g0), live(g0 + 1)

                def multiply(m):
                    dve.wait_ge(e_k, 2 * g + m + 1)
                    dve.wait_ge(e_qs, 2 * g + m + 1)
                    if g0 or m:
                        dve.wait_ge(e_s, 2 * g + m)
                    dve.scalar_tensor_tensor(out=qk[:], in0=p_k[:], scalar=bkv_c[:, m:m + 1], in1=q_sb[:],
                                             op0=ALU.add, op1=ALU.mult).then_inc(e_qk, 1)

                def maxima(m):
                    dve.wait_ge(e_s, 2 * g + m + 1)
                    dve.wait_ge(e_pen[u], 16 * h + 16)
                    if g0:
                        dve.wait_ge(e_top, 2 * g + m - 1)
                        dve.wait_ge(e_carry, 2 * g + m + 1 - KD)
                    if g0 >= 2:
                        dve.wait_ge(e_rise, 2 * g + m - 3)
                    start = top[:, 1 - u, m, GE:GE + 1] if g0 else 0.0
                    dve.tensor_tensor_scan(top[:, u, m, 1:GE + 1], pen[:, u, :], p_s[:], start, ALU.add,
                                           ALU.max).then_inc(e_top, 1)
                    if g0 == 0:
                        dve.memset(top[:, u, m, 0:1], 0.0).then_inc(e_carry, 1)
                    else:
                        dve.tensor_copy(top[:, u, m, 0:1], top[:, 1 - u, m, GE:GE + 1]).then_inc(e_carry, 1)
                    dve.wait_ge(e_carry, 2 * g + m + 1)
                    dve.wait_ge(e_top, 2 * g + m + 1)
                    if g0 or m:
                        dve.wait_ge(e_fb, 2 * g + m)
                    dve.tensor_tensor(fall_a[:], top[:, u, m, 0:GE], pen[:, u, :], ALU.add).then_inc(e_fa, 1)
                    if g0 or m:
                        dve.wait_ge(e_exp, 4 * g + 2 * m)
                    dve.tensor_tensor(rise[:], p_s[:], top[:, u, m, 1:GE + 1], ALU.subtract).then_inc(e_rise, 1)
                    dve.wait_ge(e_fa, 2 * g + m + 1)
                    dve.tensor_tensor(fall_b[:], fall_a[:], top[:, u, m, 1:GE + 1], ALU.subtract).then_inc(e_fb, 1)

                def sums(m):
                    dve.wait_ge(e_exp, 4 * g + 2 * m + 2)
                    dve.wait_ge(e_v, 2 * g + m + 1)
                    if g0 or m:
                        dve.wait_ge(e_num, 2 * g + m)
                        dve.wait_ge(e_att, 2 * g + m)
                    dve.scalar_tensor_tensor(out=pv[:], in0=p_v[m][:], scalar=bkv_c[:, KD + m:KD + m + 1],
                                             in1=prob[:], op0=ALU.add, op1=ALU.mult).then_inc(e_pv, 1)
                    if g0 or m:
                        dve.wait_ge(e_den, 2 * g + m)
                    if g0 or m:
                        dve.wait_ge(e_rd, 2 * g + m)
                        dve.wait_ge(e_att, 2 * g + m)
                    dve.tensor_tensor_scan(den[:, u, m, :], decay[:], prob[:],
                                           den[:, 1 - u, m, GE - 1:GE] if g0 else 0.0, ALU.mult,
                                           ALU.add).then_inc(e_den, 1)
                    dve.wait_ge(e_pv, 2 * g + m + 1)
                    dve.tensor_tensor_scan(num[:, u, m, :], decay[:], pv[:],
                                           num[:, 1 - u, m, GE - 1:GE] if g0 else 0.0, ALU.mult,
                                           ALU.add).then_inc(e_num, 1)
                    dve.wait_ge(e_den, 2 * g + m + 1)
                    if m == 0 and nxt:
                        low(g + 1, 1 - u, 4)
                    dve.wait_ge(e_num, 2 * g + m + 1)
                    dve.reciprocal(pv[:, 0:GE // 2], den[:, u, m, 0:GE // 2])
                    if m == 0:
                        if nxt:
                            low(g + 1, 1 - u, 5)
                        maxima(1)
                    elif live(g0 + 2):
                        low(g + 2, u, 0)
                    dve.reciprocal(pv[:, GE // 2:GE], den[:, u, m, GE // 2:GE]).then_inc(e_rd, 1)
                    if g0:
                        dve.wait_ge(e_alo, 2 * g + m - 1)
                    dve.wait_ge(e_num, 2 * g + m + 1)
                    dve.wait_ge(e_rd, 2 * g + m + 1)
                    dve.tensor_tensor(att[:, m, :], num[:, u, m, :], pv[:], ALU.mult).then_inc(e_att, 1)

                if nxt and not live(g0 - 1):
                    low(g + 1, 1 - u, 0)
                if cur:
                    multiply(0)
                if nxt:
                    low(g + 1, 1 - u, 1)
                    low(g + 1, 1 - u, 2)
                if cur:
                    maxima(0)
                if nxt:
                    low(g + 1, 1 - u, 3)
                if cur:
                    multiply(1)
                    sums(0)
                    sums(1)
                elif nxt:
                    low(g + 1, 1 - u, 4)
                    low(g + 1, 1 - u, 5)

            over_groups(dve, group)


def node_stage(nc, x, wts, ident, b1_c, b2_c, g1_c, be1_c, bo_r, g2_r, be2_r, place_of_node, attn_rows, out):
    with ExitStack() as ctx:
        def sb(name, shape, dt=F32):
            return ctx.enter_context(nc.sbuf_tensor(name, shape, dt))

        def pb(name, shape=(P, GN)):
            return ctx.enter_context(nc.psum_tensor(name, list(shape), F32))

        def sem(name):
            return ctx.enter_context(nc.semaphore(name))

        slot = sb("slot", [P, 2, J], I32)
        xt = sb("xt", [P, 2, J, D])
        z = sb("z", [P, 2, J, D])
        x2 = sb("x2", [P, 2, J, D])
        n1 = sb("n1", [P, J, D])
        h32 = sb("h32", [P, 2, KD, GN])
        h_hi = sb("h_hi", [P, 2, KD, GN], F32R)
        h_lo = sb("h_lo", [P, 2, KD, GN], F32R)
        a32 = sb("a32", [P, RING, GN])
        a_hi = sb("a_hi", [P, RING, GN], F32R)
        a_lo = sb("a_lo", [P, RING, GN], F32R)
        t_sb = sb("t_sb", [P, KD, GN])
        n2 = sb("n2", [P, J, D])
        r = sb("r", [P, 2, J, D])
        o = sb("o", [P, 2, J, D])
        st = sb("st", [P, 3 * J, 6])
        mv = sb("mv", [P, 3 * J, 2])
        var = sb("var", [P, 3 * J])
        ya = sb("ya", [P, 3 * J])
        yb = sb("yb", [P, 3 * J])
        yc = sb("yc", [P, 3 * J])
        nmr = sb("nmr", [P, 3 * J])
        p_n = [pb(f"p_n{i}") for i in range(KD)]
        p_a = [pb(f"p_a{i}") for i in range(2)]
        p_f = [pb(f"p_f{i}") for i in range(KD)]
        p_b = [pb(f"p_b{i}", (P, 2, D)) for i in range(2)]

        n_ready = sem("n_ready")
        n_slot = [sem(f"n_slot{i}") for i in range(2)]
        n_x = [sem(f"n_x{i}") for i in range(2)]
        n_z = sem("n_z")
        n_gath = [sem(f"n_gath{i}") for i in range(2)]
        n_u = sem("n_u")
        n_x2 = sem("n_x2")
        n_st = [sem(f"n_st{i}") for i in range(3)]
        n_ag = sem("n_ag")
        n_ch = sem("n_ch")
        n_n1 = sem("n_n1")
        n_tn = sem("n_tn")
        n_h32 = sem("n_h32")
        n_hhi = sem("n_hhi")
        n_hlo = sem("n_hlo")
        n_a = sem("n_a")
        n_a32 = sem("n_a32")
        n_ahi = sem("n_ahi")
        n_alo = sem("n_alo")
        n_f = sem("n_f")
        n_t = sem("n_t")
        n_tb = sem("n_tb")
        n_n2 = sem("n_n2")
        n_g2 = sem("n_g2")
        n_r = sem("n_r")
        n_o = sem("n_o")
        n_put = [sem(f"n_put{i}") for i in range(2)]
        block = ctx.enter_context(nc.Block())

        w1_hi, w1_lo = wts["1"]
        w2_hi, w2_lo = wts["2"]
        STEPS = 12

        def live(g):
            return 0 <= g < NG

        def lanes(g0):
            return TAIL if g0 == NG - 1 else P

        LOOP_END = (NG - 4) // 2

        def over_groups(eng, body):
            for g in range(-2, 6):
                body(g, g // 2, g)
            with eng.Fori(3, LOOP_END) as h:
                body(2 * h, h, 6)
                body(2 * h + 1, h, 7)
            for g in range(2 * LOOP_END, NG + 3):
                body(g, g // 2, g)

        @block.sync
        def _(sp):
            def rows_of(t, at, q):
                return t[bass.ds(at, q * J), :].rearrange("(p j) d -> p j d", j=J)

            def group(g, h, g0):
                u = g0 % 2
                moving = not isinstance(g, int)
                ahead = sp.snap(g * GN + 2 * GN) if moving else (g + 2) * GN
                behind = sp.snap(g * GN - 3 * GN) if moving else (g - 3) * GN
                n_gathered = sp.snap(16 * J * h + 16 * J) if moving else 16 * J * (h + 1)
                n_used = sp.snap(g + 1) if moving else g + 1
                n_out = sp.snap(g - 2) if moving else g - 2
                if live(g0 + 2):
                    q = lanes(g0 + 2)
                    if live(g0):
                        sp.wait_ge(n_gath[u], n_gathered)
                    sp.dma_start(slot[0:q, u, :],
                                 place_of_node[bass.ds(ahead, q * J)].rearrange("(p j) -> p j", j=J)
                                 ).then_inc(n_slot[u], 16)
                    if live(g0):
                        sp.wait_ge(n_x2, n_used)
                    sp.dma_start(xt[0:q, u, :, :], rows_of(x, ahead, q)).then_inc(n_x[u], 16)
                if live(g0 - 3):
                    q = lanes(g0 - 3)
                    sp.wait_ge(n_o, n_out)
                    sp.dma_start(rows_of(out, behind, q), o[0:q, 1 - u, :, :]).then_inc(n_put[1 - u], 16)

            over_groups(sp, group)
            for u in range(2):
                sp.wait_ge(n_put[u], 16 * ((NG + 1 - u) // 2))

        @block.gpsimd
        def _(pool):
            pool.memset(mv[:], 1.0).then_inc(n_ready, 1)

            def group(g, h, g0):
                u = g0 % 2
                if live(g0 + 2):
                    q = lanes(g0 + 2)
                    n_filled, n_placed = level(pool, g + 3), level(pool, 16 * h + 32)
                    pool.wait_ge(n_ready, 1)
                    pool.wait_ge(n_z, n_filled)
                    pool.wait_ge(n_slot[u], n_placed)
                    for j in range(J):
                        pool.indirect_dma_start(
                            z[0:q, u, j, :], None, attn_rows,
                            bass.IndirectOffsetOnAxis(ap=slot[0:q, u, j:j + 1], axis=0),
                            bounds_check=E_PAD - 1, oob_is_err=False).then_inc(n_gath[u], 16)
                if live(g0):
                    q = lanes(g0)
                    if g0 >= 2:
                        pool.wait_ge(n_r, g - 1)
                    pool.tensor_tensor(x2[0:q, u, :, :], xt[0:q, u, :, :],
                                       be2_r[0:q, :].unsqueeze(1).to_broadcast([q, J, D]), ALU.add).then_inc(n_x2, 1)
                if live(g0 + 1):
                    n = J * lanes(g0 + 1)
                    for k in range(KD):
                        pool.wait_ge(n_hhi, 2 * g + 3 + k)
                        pool.tensor_tensor(h_lo[:, 1 - u, k, 0:n], h32[:, 1 - u, k, 0:n],
                                           h_hi[:, 1 - u, k, 0:n].bitcast(F32), ALU.subtract).then_inc(n_hlo, 1)
                if live(g0 + 2):
                    q = lanes(g0 + 2)
                    pool.wait_ge(n_gath[u], 16 * J * h + 32 * J)
                    pool.wait_ge(n_x[u], 16 * h + 32)
                    pool.tensor_tensor(z[0:q, u, :, :], xt[0:q, u, :, :], z[0:q, u, :, :],
                                       ALU.add).then_inc(n_u, 1)

            over_groups(pool, group)

        @block.tensor
        def _(pe):
            def up(g, g0, f):
                n = J * lanes(g0)
                if f == 0:
                    pe.wait_ge(n_hhi, 2 * g + 2)
                if not (isinstance(g, int) and g == 0 and f < 2):
                    pe.wait_ge(n_a32, NF * g + f - 1)
                u = g0 % 2
                for k in range(KD):
                    hi, lo = w1_hi[:, k, f * P:(f + 1) * P], w1_lo[:, k, f * P:(f + 1) * P]
                    pe.matmul(p_a[f % 2][:, 0:n], hi, h_hi[:, u, k, 0:n], start=(k == 0), stop=False)
                    pe.matmul(p_a[f % 2][:, 0:n], lo, h_hi[:, u, k, 0:n], start=False, stop=False)
                if f == 0:
                    pe.wait_ge(n_hlo, 2 * g + 2)
                for k in range(KD):
                    mm = pe.matmul(p_a[f % 2][:, 0:n], w1_hi[:, k, f * P:(f + 1) * P], h_lo[:, u, k, 0:n],
                                   start=False, stop=(k == KD - 1))
                mm.then_inc(n_a, 1)

            def down(g, g0, f):
                n = J * lanes(g0)
                pe.wait_ge(n_ahi, NF * g + f + 1)
                s = f % RING
                for m in range(KD):
                    if f == 0 and g0 >= 1:
                        pe.wait_ge(n_t, 2 * g - 1 + m)
                    pe.matmul(p_f[m][:, 0:n], w2_hi[:, f, m * P:(m + 1) * P], a_hi[:, s, 0:n],
                              start=(f == 0), stop=False)
                    pe.matmul(p_f[m][:, 0:n], w2_lo[:, f, m * P:(m + 1) * P], a_hi[:, s, 0:n],
                              start=False, stop=False)
                pe.wait_ge(n_alo, NF * g + f + 1)
                for m in range(KD):
                    mm = pe.matmul(p_f[m][:, 0:n], w2_hi[:, f, m * P:(m + 1) * P], a_lo[:, s, 0:n],
                                   start=False, stop=(f == NF - 1))
                mm.then_inc(n_f, 1)

            def turn_back(g, g0):
                q = lanes(g0)
                pe.wait_ge(n_t, 2 * g + 2)
                if g0 >= 1:
                    pe.wait_ge(n_n2, g)
                for j in range(J):
                    for m in range(KD):
                        mm = pe.transpose(p_b[j // 2][0:q, j % 2, m * P:(m + 1) * P],
                                          t_sb[:, m, j * q:(j + 1) * q], ident[:])
                    if j % 2:
                        mm.then_inc(n_tb, 1)

            def turn(g, g0):
                q = lanes(g0)
                pe.wait_ge(n_n1, g + 1)
                if g0 >= 1:
                    pe.wait_ge(n_h32, 2 * g)
                for k in range(KD):
                    for j in range(J):
                        mm = pe.transpose(p_n[k][:, j * q:(j + 1) * q], n1[0:q, j, k * P:(k + 1) * P],
                                          ident[0:q, 0:q])
                    mm.then_inc(n_tn, 1)

            def group(g, h, g0):
                for f in range(NF):
                    if live(g0):
                        up(g, g0, f)
                    if live(g0 + 1) and f == 2:
                        turn(g + 1, g0 + 1)
                    if live(g0) and f >= 2:
                        down(g, g0, f - 2)
                    if live(g0 - 1) and f < 2:
                        down(g - 1, g0 - 1, f + NF - 2)
                    if live(g0 - 1) and f == 4:
                        turn_back(g - 1, g0 - 1)

            over_groups(pe, group)

        @block.scalar
        def _(act):
            def group(g, h, g0):
                u = g0 % 2
                if live(g0 + 2):
                    q = lanes(g0 + 2)
                    if live(g0):
                        act.wait_ge(n_n1, g + 1)
                    act.activation(z[0:q, u, :, :], bo_r[0:q, :].unsqueeze(1).to_broadcast([q, J, D]),
                                   ACT.Copy).then_inc(n_z, 1)
                for f in range(NF):
                    if live(g0):
                        n = J * lanes(g0)
                        s = f % RING
                        free = not (isinstance(g, int) and g == 0 and f < RING)
                        act.wait_ge(n_a, NF * g + f + 1)
                        if free:
                            act.wait_ge(n_alo, NF * g + f + 1 - RING)
                        act.activation(a32[:, s, 0:n], p_a[f % 2][:, 0:n], ACT.Gelu,
                                       bias=b1_c[:, f:f + 1]).then_inc(n_a32, 1)
                        if free:
                            act.wait_ge(n_f, NF * g + f + 1 - RING)
                        act.wait_ge(n_a32, NF * g + f + 1)
                        act.activation(a_hi[:, s, 0:n], a32[:, s, 0:n], ACT.Copy).then_inc(n_ahi, 1)
                    if f == 1 and live(g0 - 2):
                        q = lanes(g0 - 2)
                        act.wait_ge(n_ch, STEPS * g + 2 * STEPS)
                        if g0 >= 3:
                            act.wait_ge(n_g2, g - 2)
                        for j in range(J):
                            a = act.activation(n2[0:q, j, :], p_b[j // 2][0:q, j % 2, :], ACT.Identity,
                                               bias=nmr[0:q, J + j:J + j + 1], scale=ya[0:q, J + j:J + j + 1])
                        a.then_inc(n_n2, 1)
                    if f == 3 and live(g0 - 3):
                        q = lanes(g0 - 3)
                        act.wait_ge(n_ch, STEPS * g + 2 * STEPS)
                        if g0 >= 5:
                            act.wait_ge(n_put[1 - u], 16 * h - 32 + 16 * u)
                        for j in range(J):
                            a = act.activation(o[0:q, 1 - u, j, :], r[0:q, 1 - u, j, :], ACT.Identity,
                                               bias=nmr[0:q, 2 * J + j:2 * J + j + 1],
                                               scale=ya[0:q, 2 * J + j:2 * J + j + 1])
                        a.then_inc(n_o, 1)
                    if f == 4 and live(g0 + 1):
                        n = J * lanes(g0 + 1)
                        for k in range(KD):
                            act.wait_ge(n_h32, 2 * g + 3 + k)
                            if g0 >= 1:
                                act.wait_ge(n_a, NF * g)
                            act.activation(h_hi[:, 1 - u, k, 0:n], h32[:, 1 - u, k, 0:n],
                                           ACT.Copy).then_inc(n_hhi, 1)

            over_groups(act, group)

        @block.vector
        def _(dve):
            def low(g, g0, f):
                n = J * lanes(g0)
                s = f % RING
                dve.wait_ge(n_ahi, NF * g + f + 1)
                if not (isinstance(g, int) and g == 0 and f < RING):
                    dve.wait_ge(n_f, NF * g + f + 1 - RING)
                dve.tensor_tensor(a_lo[:, s, 0:n], a32[:, s, 0:n], a_hi[:, s, 0:n].bitcast(F32),
                                  ALU.subtract).then_inc(n_alo, 1)

            def residual(g, g0):
                u, n = g0 % 2, J * lanes(g0)
                dve.wait_ge(n_f, NF * g + NF)
                dve.wait_ge(n_h32, 2 * g + 2)
                if g0 >= 1:
                    dve.wait_ge(n_tb, 2 * g)
                for m in range(KD):
                    dve.scalar_tensor_tensor(out=t_sb[:, m, 0:n], in0=p_f[m][:, 0:n], scalar=b2_c[:, m:m + 1],
                                             in1=h32[:, u, m, 0:n], op0=ALU.add, op1=ALU.add).then_inc(n_t, 1)

            def first_statistics(g, g0):
                u, q = g0 % 2, lanes(g0)
                dve.wait_ge(n_u, g + 1)
                if g0 >= 1:
                    dve.wait_ge(n_ag, g)
                for j in range(J):
                    op = dve.bn_stats(st[0:q, j, :], z[0:q, u, j, :])
                op.then_inc(n_st[0], 1)

            def second_statistics(g, g0):
                q = lanes(g0)
                dve.wait_ge(n_tb, 2 * g + 2)
                for j in range(J):
                    op = dve.bn_stats(st[0:q, J + j, :], p_b[j // 2][0:q, j % 2, :])
                op.then_inc(n_st[1], 1)

            def norms(g, g0):
                u = g0 % 2
                there = (live(g0 + 1), live(g0 - 2), live(g0 - 3))
                there_at = [level(dve, v) if t else 0 for v, t in zip((g + 2, g - 1, g - 2), there)]
                chained = level(dve, STEPS * g + STEPS)
                dve.wait_ge(n_ready, 1)
                for i in range(3):
                    if there[i]:
                        dve.wait_ge(n_st[i], there_at[i])
                if g0 > -1:
                    dve.wait_ge(n_ch, chained)
                for i, q0 in enumerate((g0 + 1, g0 - 2, g0 - 3)):
                    if there[i]:
                        q = lanes(q0)
                        for j in range(i * J, (i + 1) * J):
                            op = dve.bn_aggr(mv[0:q, j, :], st[0:q, j, :])
                op.then_inc(n_ag, 1)
                dve.wait_ge(n_ag, g + 2)
                if live(g0 - 3):
                    dve.wait_ge(n_n2, g - 2)
                if live(g0 - 4):
                    dve.wait_ge(n_o, g - 3)
                base = STEPS * g + STEPS
                dve.tensor_scalar(var[:], mv[:, :, 1], EPS, None, ALU.add).then_inc(n_ch, 1)
                dve.wait_ge(n_ch, base + 1)
                dve.tensor_scalar(ya[:].bitcast(I32), var[:].bitcast(I32), -0.5, float(0x5F3759DF), ALU.mult,
                                  ALU.add).then_inc(n_ch, 1)
                for i in range(3):
                    dve.wait_ge(n_ch, base + 2 + 3 * i)
                    dve.scalar_tensor_tensor(out=yb[:], in0=ya[:], scalar=-0.5, in1=ya[:], op0=ALU.mult,
                                             op1=ALU.mult).then_inc(n_ch, 1)
                    if i == 0 and live(g0 - 1):
                        low(g - 1, g0 - 1, NF - 1)
                    if i == 2 and live(g0):
                        low(g, g0, 0)
                    dve.wait_ge(n_ch, base + 3 + 3 * i)
                    dve.tensor_tensor(yc[:], yb[:], var[:], ALU.mult).then_inc(n_ch, 1)
                    dve.wait_ge(n_ch, base + 4 + 3 * i)
                    dve.scalar_tensor_tensor(out=ya[:], in0=yc[:], scalar=1.5, in1=ya[:], op0=ALU.add,
                                             op1=ALU.mult).then_inc(n_ch, 1)
                dve.wait_ge(n_ch, base + STEPS - 1)
                dve.scalar_tensor_tensor(out=nmr[:], in0=mv[:, :, 0], scalar=-1.0, in1=ya[:], op0=ALU.mult,
                                         op1=ALU.mult).then_inc(n_ch, 1)
                dve.wait_ge(n_ch, base + STEPS)
                if there[0]:
                    q = lanes(g0 + 1)
                    if live(g0):
                        dve.wait_ge(n_tn, 2 * g + 2)
                    for j in range(J):
                        op = dve.tensor_scalar(n1[0:q, j, :], z[0:q, 1 - u, j, :], ya[0:q, j:j + 1],
                                               nmr[0:q, j:j + 1], ALU.mult, ALU.add)
                    op.then_inc(n_n1, 1)

            def first_out(g, g0):
                u, n = g0 % 2, J * lanes(g0)
                if g0 >= 2:
                    dve.wait_ge(n_hlo, 2 * g - 2)
                    dve.wait_ge(n_t, 2 * g - 2)
                for k in range(KD):
                    dve.wait_ge(n_tn, 2 * g + 1 + k)
                    dve.tensor_scalar(h32[:, u, k, 0:n], p_n[k][:, 0:n], g1_c[:, k:k + 1], be1_c[:, k:k + 1],
                                      ALU.mult, ALU.add).then_inc(n_h32, 1)

            def close(g, g0):
                u, q = g0 % 2, lanes(g0)
                dve.wait_ge(n_n2, g + 1)
                if g0 >= 2:
                    dve.wait_ge(n_o, g - 1)
                dve.wait_ge(n_ag, g + 4)
                dve.tensor_tensor(r[0:q, u, :, :], n2[0:q, :, :],
                                  g2_r[0:q, :].unsqueeze(1).to_broadcast([q, J, D]), ALU.mult).then_inc(n_g2, 1)
                dve.wait_ge(n_g2, g + 1)
                dve.wait_ge(n_x2, g + 1)
                dve.tensor_tensor(r[0:q, u, :, :], r[0:q, u, :, :], x2[0:q, u, :, :], ALU.add).then_inc(n_r, 1)
                dve.wait_ge(n_r, g + 1)
                for j in range(J):
                    op = dve.bn_stats(st[0:q, 2 * J + j, :], r[0:q, u, j, :])
                op.then_inc(n_st[2], 1)

            def group(g, h, g0):
                if g0 > -2:
                    norms(g, g0)
                for f in range(NF):
                    if live(g0) and f not in (0, NF - 1):
                        low(g, g0, f)
                    if f == 1 and live(g0 - 1):
                        residual(g - 1, g0 - 1)
                    if f == 2 and live(g0 - 2):
                        close(g - 2, g0 - 2)
                    if f == 3 and live(g0 + 1):
                        first_out(g + 1, g0 + 1)
                    if f == 4 and live(g0 - 1):
                        second_statistics(g - 1, g0 - 1)
                    if f == 6 and live(g0 + 2):
                        first_statistics(g + 2, g0 + 2)

            over_groups(dve, group)


_INS = ['x', 'src', 'dst', 'edge_attr_256', 'L0_gnn_Wq_w', 'L0_gnn_Wq_b', 'L0_gnn_Wkv_w', 'L0_gnn_Wkv_b',
        'L0_gnn_Wo_w', 'L0_gnn_Wo_b', 'L0_gnn_ln1_g', 'L0_gnn_ln1_b', 'L0_gnn_ffn1_w', 'L0_gnn_ffn1_b',
        'L0_gnn_ffn2_w', 'L0_gnn_ffn2_b', 'L0_gnn_ln2_g', 'L0_gnn_ln2_b']


def kernel(**inputs):
    import numpy as _np
    import concourse.bacc as _bacc
    from concourse import mybir as _mybir
    from concourse.bass_utils import run_bass_kernel_spmd as _run

    nc = _bacc.Bacc("TRN2", target_bir_lowering=False, num_devices=1)
    arrays, args = {}, []
    for name in _INS:
        a = _np.ascontiguousarray(inputs[name])
        arrays[f"in_{name}_dram"] = a
        args.append(nc.dram_tensor(f"in_{name}_dram", a.shape, _mybir.dt.from_np(a.dtype), kind="ExternalInput").ap())
    out = nc.dram_tensor("out_dram", (N_NODES, D), F32, kind="ExternalOutput").ap()
    build(nc, *args, out)
    r = _run(nc, [arrays], core_ids=[0])
    return r.results[0]["out_dram"]
```
